# Optimizing a Trainium2 kernel written in Bass

```python
import numpy as np
import jax
import jax.numpy as jnp

def _softmax(x, axis=-1):
    return jax.nn.softmax(x, axis=axis)

def _gelu(x):
    return jax.nn.gelu(x, approximate=True)

def _silu(x):
    return jax.nn.silu(x)

def _sigmoid(x):
    return jax.nn.sigmoid(x)

def _layernorm(x, axis=-1, eps=1e-05):
    m = jnp.mean(x, axis=axis, keepdims=True)
    v = jnp.var(x, axis=axis, keepdims=True)
    return (x - m) / jnp.sqrt(v + eps)

def _scatter_add(tgt, idx, src, axis=0):
    return tgt.at[idx].add(src)

def _segment_sum(src, seg, n):
    return jax.ops.segment_sum(src, seg, n)
kernel_name = 'mk_conv_preact_d1_conv_nchw128_r4_928f8c'

def setup_inputs(seed: int=0):
    np.random.seed(seed)
    _w = jnp.asarray

    def _rec_inputs():
        import jax
        import jax.numpy as jnp
        _gk = jax.random.key(seed)
        x = -7.109e-05 + 0.9999 * jax.random.normal(jax.random.fold_in(_gk, 1), (8, 32, 64, 64), jnp.float32)
        return x
    x = _rec_inputs()

    def _L0_conv_setup():
        import jax, jax.numpy as jnp
        import numpy as np
        B, C, H, W = (8, 32, 64, 64)
        KERNELS = [1, 3, 5]

        def _dwconv(x, w, k):
            return jax.lax.conv_general_dilated(x, w, window_strides=(1, 1), padding=[(k // 2, k // 2), (k // 2, k // 2)], dimension_numbers=('NCHW', 'OIHW', 'NCHW'), feature_group_count=x.shape[1])
        key = jax.random.key(seed)
        ks = jax.random.split(key, 5)
        x = jax.random.normal(ks[0], (B, C, H, W), jnp.float32)
        w1 = jax.random.normal(ks[1], (4 * C, 1, 1, 1), jnp.float32) * 0.2
        w3 = jax.random.normal(ks[2], (4 * C, 1, 3, 3), jnp.float32) * 0.1
        w5 = jax.random.normal(ks[3], (4 * C, 1, 5, 5), jnp.float32) * 0.05
        w_proj = jax.random.normal(ks[4], (4 * C, 12 * C, 1, 1), jnp.float32) * 0.02
        return {'x': x, 'w1': w1, 'w3': w3, 'w5': w5, 'w_proj': w_proj}
    _L0_conv_all = _L0_conv_setup()
    _L0_conv_in = {k: v for k, v in _L0_conv_all.items() if k in ('w1', 'w3', 'w5', 'w_proj')}
    del _L0_conv_all
    return {'x': x, 'L0_conv_w1': _L0_conv_in['w1'], 'L0_conv_w3': _L0_conv_in['w3'], 'L0_conv_w5': _L0_conv_in['w5'], 'L0_conv_w_proj': _L0_conv_in['w_proj']}

def reference(x, L0_conv_w1, L0_conv_w3, L0_conv_w5, L0_conv_w_proj):
    import jax
    import jax.numpy as jnp

    def _L0_conv_ref(x, w1, w3, w5, w_proj):
        import jax, jax.numpy as jnp
        import numpy as np
        B, C, H, W = (8, 32, 64, 64)
        KERNELS = [1, 3, 5]

        def _dwconv(x, w, k):
            return jax.lax.conv_general_dilated(x, w, window_strides=(1, 1), padding=[(k // 2, k // 2), (k // 2, k // 2)], dimension_numbers=('NCHW', 'OIHW', 'NCHW'), feature_group_count=x.shape[1])
        xd = jnp.concatenate([x[:, :, 0::2, 0::2], x[:, :, 0::2, 1::2], x[:, :, 1::2, 0::2], x[:, :, 1::2, 1::2]], axis=1)
        feats = jnp.concatenate([_dwconv(xd, w1, 1), _dwconv(xd, w3, 3), _dwconv(xd, w5, 5)], axis=1)
        y = jnp.einsum('bchw,oc->bohw', feats, w_proj[:, :, 0, 0])
        c = y.shape[1] // 4
        ll, lh, hl, hh = jnp.split(y, 4, axis=1)
        out = jnp.zeros((y.shape[0], c, y.shape[2] * 2, y.shape[3] * 2), y.dtype)
        out = out.at[:, :, 0::2, 0::2].set(ll).at[:, :, 0::2, 1::2].set(lh).at[:, :, 1::2, 0::2].set(hl).at[:, :, 1::2, 1::2].set(hh)
        return out

    def _gn(v, G=32, eps=1e-05):
        B_, C_, H_, W_ = v.shape
        g = v.reshape(B_, G, C_ // G, H_, W_)
        m = jnp.mean(g, axis=(2, 3, 4), keepdims=True)
        s = jnp.var(g, axis=(2, 3, 4), keepdims=True)
        return ((g - m) / jnp.sqrt(s + eps)).reshape(v.shape)

    def _ln_c(v, eps=1e-06):
        m = jnp.mean(v, axis=1, keepdims=True)
        s = jnp.var(v, axis=1, keepdims=True)
        return (v - m) / jnp.sqrt(s + eps)

    def _ln_t(v, eps=1e-05):
        m = jnp.mean(v, axis=-1, keepdims=True)
        s = jnp.var(v, axis=-1, keepdims=True)
        return (v - m) / jnp.sqrt(s + eps)

    def _to_tokens(v):
        B_, C_, H_, W_ = v.shape
        return v.reshape(B_, C_, H_ * W_).transpose(0, 2, 1)

    def _from_tokens(t, like):
        B_, C_, H_, W_ = like.shape
        return t.transpose(0, 2, 1).reshape(B_, C_, H_, W_)
    x = x + _L0_conv_ref(_gn(x), L0_conv_w1, L0_conv_w3, L0_conv_w5, L0_conv_w_proj)
    return x

_drawn_inputs = setup_inputs


def setup_inputs(seed=0):
    import zlib

    import numpy as np

    out = dict(_drawn_inputs(seed))
    spreads = {}
    factors = {}
    for name, (base, spread) in spreads.items():
        noise = np.random.default_rng([zlib.crc32(name.encode()), seed]).standard_normal(out[name].shape)
        drawn = base * np.exp(spread * noise) if base else spread * noise
        out[name] = jnp.asarray(drawn.astype(out[name].dtype))
    for name, factor in factors.items():
        out[name] = (out[name] * factor).astype(out[name].dtype)
    return out
```

```python
from contextlib import ExitStack

import concourse.bass as bass
from concourse import mybir

ALU = mybir.AluOpType
ACT = mybir.ActivationFunctionType
F32 = mybir.dt.float32
F32R = mybir.dt.float32r

B, C, H, W = 8, 32, 64, 64
PH, PW = H // 2, W // 2
P = 4 * C
HALF = P // 2
PAIRS = B // 2
EPS = 1e-5
BANK_ROWS = 512 // PW
BANKS = PH // BANK_ROWS

PITCH = PW + 2
G_ROWS = PH + 4
G_SIZE = G_ROWS * PITCH + 4
S_SIZE = PH * PITCH + 4

INNER = [(0, 0)] + [(dy, dx) for dy in (-1, 0, 1) for dx in (-1, 0, 1) if (dy, dx) != (0, 0)]
PE_RING = [(2, 2)]
POOL_TAPS = [(0, 2), (-2, -2), (-2, 2), (2, -2)]
RING = [(dy, dx) for dy in range(-2, 3) for dx in range(-2, 3) if max(abs(dy), abs(dx)) == 2]
DVE_FIRST, DVE_LAST = (0, -2), (0, -2)
_rest = [t for t in RING if t not in PE_RING + POOL_TAPS + [DVE_FIRST]]
DVE_TAPS = [DVE_FIRST] + _rest
PE_TAPS = INNER + PE_RING
N_INNER, N_PE, N_DVE = len(INNER), len(PE_TAPS), len(DVE_TAPS)
N_PROD = len(POOL_TAPS) - 1
N_STEP = N_DVE - 1


def w5_col(tap):
    return (tap[0] + 2) * 5 + tap[1] + 2


W3_AT, W1_AT = 25, 34
N_COEF = 35


def w3_col(tap):
    return W3_AT + (tap[0] + 1) * 3 + tap[1] + 1


def span(d, lo, hi):
    return max(lo, -d), min(hi, PH - d)


def build(nc, x, w1, w3, w5, wp, out):
    with ExitStack() as ctx:
        def sb(name, shape, dt):
            return ctx.enter_context(nc.sbuf_tensor(name, shape, dt))

        def ps(name, shape):
            return ctx.enter_context(nc.psum_tensor(name, shape, F32))

        def sem(name):
            return ctx.enter_context(nc.semaphore(name))

        X = sb("X", [P, PAIRS, PH, W], F32)
        Y = sb("Y", [P, PH, PW, 2], F32)
        G = sb("G", [P, 2, G_SIZE], F32)
        HI = sb("HI", [P, 2, S_SIZE], F32R)
        LO = sb("LO", [P, 2, S_SIZE], F32R)
        PSUMED = sb("POOLSUM", [P, 2, PH, PW], F32)
        PROD = sb("PROD", [P, N_PROD, PH * PW], F32)
        F = sb("F", [P, 2, PH * PW], F32)
        wp_sb = sb("wp_sb", [P, 3 * P], F32)
        w_sb = sb("w_sb", [P, N_COEF], F32)
        coef = sb("coef", [P, N_COEF], F32)
        wpT = sb("wpT", [P, 3, P], F32)
        weff = sb("weff", [P, N_PE, P], F32)
        whi = sb("whi", [P, N_PE, P], F32R)
        wlo = sb("wlo", [P, N_PE, P], F32R)
        ident = sb("ident", [P, P], F32)
        ident_ph = sb("ident_ph", [P, P], F32)
        wp_ph = sb("wp_ph", [P, 3, P], F32)
        avg = sb("avg", [P, P], F32)
        mhalf = sb("mhalf", [P, PAIRS], F32)
        st = sb("st", [P, PAIRS, 4, 6], F32)
        agg = sb("agg", [P, PAIRS, 2], F32)
        dev = sb("dev", [P, PAIRS], F32)
        dev2 = sb("dev2", [P, PAIRS], F32)
        vare = sb("vare", [P, PAIRS], F32)
        rstd = sb("rstd", [P, PAIRS], F32)
        nbias = sb("nbias", [P, PAIRS], F32)

        YP = ps("YP", [P, 2, PH * PW])
        ACC = ps("ACC", [P, PH, PW])
        WT_PS = ps("WT_PS", [P, 512])
        SMALL = ps("SMALL", [P, 512])
        COEF_PS = SMALL[:, 0:N_COEF]
        COMB = SMALL[:, 40:40 + 2 * PAIRS].rearrange("p (t s) -> p t s", s=2)

        x_loaded = [sem(f"x_loaded{t}") for t in range(PAIRS)]
        wp_loaded, w_loaded = sem("wp_loaded"), sem("w_loaded")
        const_step, pads_zero = sem("const_step"), sem("pads_zero")
        permuted = sem("permuted")
        wt_ready, coef_ready = sem("wt_ready"), sem("coef_ready")
        wpT_ready, coef_copied = sem("wpT_ready"), sem("coef_copied")
        w5_scaled, weff_step = sem("w5_scaled"), sem("weff_step")
        whi_ready, wlo_ready = sem("whi_ready"), sem("wlo_ready")
        bn_done, agg_done, comb_done = sem("bn_done"), sem("agg_done"), sem("comb_done")
        stat_step, rstd_done, stats_ready = sem("stat_step"), sem("rstd_done"), sem("stats_ready")
        stat_step_in = sem("stat_step_in")
        g_ready, hi_ready, lo_ready = sem("g_ready"), sem("hi_ready"), sem("lo_ready")
        first_prod, prod_ready, prod_added = sem("first_prod"), sem("prod_ready"), sem("prod_added")
        acc_step, acc0_done, f_ready = sem("acc_step"), sem("acc0_done"), sem("f_ready")
        inner_done, conv_done, y_copied = sem("inner_done"), sem("conv_done"), sem("y_copied")
        row_added, last_added, stored = sem("row_added"), sem("last_added"), sem("stored")

        def g_image(par):
            return G[:, par, 2 * PITCH:2 * PITCH + PH * PITCH].rearrange("p (r c) -> p r c", c=PITCH)[:, :, 2:PITCH]

        def g_tap(par, tap, full=False):
            dy, dx = tap
            at = (2 + dy) * PITCH + 2 + dx
            v = G[:, par, at:at + PH * PITCH].rearrange("p (r c) -> p r c", c=PITCH)[:, :, 0:PW]
            (r0, r1), (c0, c1) = ((0, PH), (0, PW)) if full else (span(dy, 0, PH), span(dx, 0, PW))
            return v[:, r0:r1, c0:c1]

        def part(tile, tap):
            (r0, r1), (c0, c1) = span(tap[0], 0, PH), span(tap[1], 0, PW)
            return tile[:, r0:r1, c0:c1]

        def prod(k):
            (r0, r1), (c0, c1) = span(POOL_TAPS[k + 1][0], 0, PH), span(POOL_TAPS[k + 1][1], 0, PW)
            return PROD[:, k, 0:(r1 - r0) * (c1 - c0)].rearrange("p (r c) -> p r c", c=c1 - c0)

        def s_image(tile, par):
            return tile[:, par, 0:PH * PITCH].rearrange("p (r c) -> p r c", c=PITCH)[:, :, 2:PITCH]

        def of5(tap):
            return coef[:, w5_col(tap):w5_col(tap) + 1]

        block = ctx.enter_context(nc.Block())

        def load_x(eng, b):
            for i in range(2):
                p0 = HALF * (b % 2) + C * i
                src = x[b].rearrange("c (h i) w -> i c h w", i=2)[i]
                eng.dma_start(X[p0:p0 + C, b // 2, :, :], src).then_inc(x_loaded[b // 2], 16)

        @block.sync
        def _(sp):
            load_x(sp, 0)
            for b in range(2, B):
                load_x(sp, b)

            def store(t, par, half):
                r0 = half * BANK_ROWS
                for i in range(2):
                    p0 = HALF * par + C * i
                    dst = out[bass.ds(2 * t + par, 1)].rearrange("b c (h i) w -> i (b c) h w", i=2)[i]
                    src = X[p0:p0 + C, bass.ds(t, 1), r0:r0 + BANK_ROWS, :].rearrange("p t h w -> p (t h) w")
                    sp.dma_start(dst[:, r0:r0 + BANK_ROWS, :], src).then_inc(stored, 16)

            with sp.Fori(0, PAIRS - 1) as t:
                for half in range(2):
                    sp.wait_ge(row_added, 2 * t + half + 1)
                    for par in range(2):
                        store(t, par, half)
            for half in range(2):
                sp.wait_ge(row_added, B - 2 + half + 1)
                store(PAIRS - 1, 0, half)
            for half in range(2):
                sp.wait_ge(last_added, 2 * half + 2)
                store(PAIRS - 1, 1, half)
            sp.wait_ge(stored, 16 * 2 * 2 * B)

        @block.gpsimd
        def _(pool):
            pool.memset(ident[:, :], 0.0).then_inc(const_step, 1)
            pool.memset(avg[:, :], 0.0).then_inc(const_step, 1)
            pool.wait_ge(const_step, 2)
            pool.affine_select(out=ident[:, :], in_=ident[:, :], compare_op=ALU.not_equal, fill=1.0,
                               base=0, pattern=[[-1, P]], channel_multiplier=1).then_inc(const_step, 1)
            pool.affine_select(out=avg[:, :], in_=avg[:, :], compare_op=ALU.not_equal, fill=0.5,
                               base=0, pattern=[[-1, P]], channel_multiplier=1).then_inc(const_step, 1)
            a = avg[:, :].rearrange("p (b i c) -> p b i c", b=2, i=2)
            for i in range(2):
                pool.wait_ge(const_step, 4 + i)
                pool.affine_select(out=a[:, :, i, :], in_=a[:, :, i, :], compare_op=ALU.not_equal, fill=0.5,
                                   base=-C * (1 - i), pattern=[[-HALF, 2], [-1, C]],
                                   channel_multiplier=1).then_inc(const_step, 1)
            pool.memset(mhalf[:, :], -0.5).then_inc(const_step, 1)
            for tile in (HI, LO):
                v = tile[:, :, 0:PH * PITCH].rearrange("p b (r c) -> p b r c", c=PITCH)
                pool.memset(v[:, :, :, 0:2].bitcast(F32), 0.0).then_inc(pads_zero, 1)
                pool.memset(tile[:, :, PH * PITCH:S_SIZE].bitcast(F32), 0.0).then_inc(pads_zero, 1)
            v = G[:, :, 0:G_ROWS * PITCH].rearrange("p b (r c) -> p b r c", c=PITCH)
            pool.memset(v[:, :, 2:PH + 2, 0:2], 0.0).then_inc(pads_zero, 1)
            pool.memset(G[:, :, 0:2 * PITCH], 0.0).then_inc(pads_zero, 1)
            pool.memset(G[:, :, (PH + 2) * PITCH:G_SIZE], 0.0).then_inc(pads_zero, 1)

            def inv_std(n, a, b):
                pool.wait_ge(const_step, 7)
                pool.wait_ge(stat_step, n)
                pool.tensor_tensor(rstd[:, a:b], vare[:, a:b], mhalf[:, a:b], ALU.pow).then_inc(rstd_done, 1)

            def prepare(b, par, first=False):
                pool.wait_ge(hi_ready, b + 1)
                if not first:
                    pool.wait_ge(inner_done, b - 1)
                pool.tensor_tensor(s_image(LO, par), g_image(par), s_image(HI, par).bitcast(F32),
                                   ALU.subtract).then_inc(lo_ready, 1)
                pool.wait_ge(first_prod, b + 1)
                for k in range(N_PROD):
                    pool.wait_ge(prod_ready, N_PROD * b + k + 1)
                    if k > 0:
                        pool.wait_ge(prod_added, N_PROD * b + k)
                    dst = part(PSUMED[:, par, :, :], POOL_TAPS[k + 1])
                    pool.tensor_tensor(dst, dst, prod(k), ALU.add).then_inc(prod_added, 1)

            def residual(t, p1, half, need):
                r0 = half * BANK_ROWS
                pool.wait_ge(y_copied, need)
                xr = X[0:p1, bass.ds(t, 1), r0:r0 + BANK_ROWS, :].rearrange("p t h w -> p (t h w)")
                yr = Y[0:p1, r0:r0 + BANK_ROWS, :, :].rearrange("p h w j -> p (h w j)")
                pool.tensor_tensor(xr, xr, yr, ALU.add).then_inc(row_added, 1)

            inv_std(1, 0, 1)
            prepare(0, 0, True)
            inv_std(2, 1, PAIRS)
            prepare(1, 1, True)
            prepare(2, 0)
            with pool.Fori(0, PAIRS - 2) as t:
                prepare(2 * t + 3, 1)
                for half in range(2):
                    residual(t, P, half, 4 * t + 4)
                prepare(2 * t + 4, 0)
            prepare(B - 1, 1)
            for half in range(2):
                residual(PAIRS - 2, P, half, 2 * (B - 2))
            for half in range(2):
                residual(PAIRS - 1, HALF, half, 2 * (B - 1))

        @block.scalar
        def _(act):
            act.dma_start(wp_sb[:, :], wp.rearrange("o c a b -> o (c a b)")).then_inc(wp_loaded, 16)
            act.dma_start(w_sb[:, 0:W3_AT], w5.rearrange("c a h w -> c (a h w)")).then_inc(w_loaded, 16)
            act.dma_start(w_sb[:, W3_AT:W1_AT], w3.rearrange("c a h w -> c (a h w)")).then_inc(w_loaded, 16)
            act.dma_start(w_sb[:, W1_AT:N_COEF], w1.rearrange("c a h w -> c (a h w)")).then_inc(w_loaded, 16)
            load_x(act, 1)
            act.wait_ge(wt_ready, 1)
            for k in range(3):
                act.activation(wpT[:, k, :].rearrange("p (j i o) -> p j i o", j=2, i=2),
                               WT_PS[:, k * P:(k + 1) * P].rearrange("p (i j o) -> p j i o", j=2, i=2),
                               ACT.Copy).then_inc(wpT_ready, 1)
            act.wait_ge(wpT_ready, 3)
            act.wait_ge(coef_copied, 1)
            for n, tap in enumerate(PE_TAPS):
                act.activation(weff[:, n, :], wpT[:, 2, :], ACT.Copy, scale=of5(tap)).then_inc(w5_scaled, 1)

            def prepare(b, par, t, first=False):
                if not first:
                    act.wait_ge(f_ready, b - 1)
                    act.wait_ge(lo_ready, b - 1)
                p0 = HALF * par
                rows = X[p0:p0 + HALF, bass.ds(t, 1), :, :].rearrange("p t h (w j) -> p (t h) w j", j=2)
                for j in range(2):
                    act.activation(g_image(par)[HALF * j:HALF * (j + 1)], rows[:, :, :, j], ACT.Identity,
                                   bias=nbias[p0:p0 + HALF, bass.ds(t, 1)],
                                   scale=rstd[p0:p0 + HALF, bass.ds(t, 1)]).then_inc(g_ready, 1)
                act.wait_ge(g_ready, 2 * b + 2)
                if not first:
                    act.wait_ge(inner_done, b - 1)
                act.activation(s_image(HI, par), g_image(par), ACT.Copy).then_inc(hi_ready, 1)

            def products(b, par, first=False):
                act.activation(PSUMED[:, par, :, :], g_tap(par, POOL_TAPS[0], True), ACT.Copy,
                               scale=of5(POOL_TAPS[0])).then_inc(first_prod, 1)
                for k in range(N_PROD):
                    if not first:
                        act.wait_ge(prod_added, N_PROD * (b - 1) + k + 1)
                    act.activation(prod(k), g_tap(par, POOL_TAPS[k + 1]), ACT.Copy,
                                   scale=of5(POOL_TAPS[k + 1])).then_inc(prod_ready, 1)

            def copy_y(b, par, free=None):
                act.wait_ge(conv_done, b + 1)
                if free is not None:
                    act.wait_ge(row_added, free)
                for j in range(2):
                    act.activation(Y[HALF * par:HALF * (par + 1), :, :, j],
                                   YP[HALF * j:HALF * (j + 1), par, :].rearrange("p (h w) -> p h w", w=PW),
                                   ACT.Copy).then_inc(y_copied, 1)

            act.wait_ge(pads_zero, 7)
            act.wait_ge(stats_ready, 1)
            prepare(0, 0, 0, True)
            act.wait_ge(weff_step, N_INNER + 1)
            act.wait_ge(w5_scaled, N_PE)
            act.activation(whi[:, :, :], weff[:, :, :], ACT.Copy).then_inc(whi_ready, 1)
            products(0, 0, True)
            act.wait_ge(stats_ready, 2)
            prepare(1, 1, 0, True)
            products(1, 1)
            with act.Fori(0, PAIRS - 1) as t:
                prepare(2 * t + 2, 0, t + 1)
                products(2 * t + 2, 0)
                copy_y(2 * t, 0, 2 * t)
                prepare(2 * t + 3, 1, t + 1)
                products(2 * t + 3, 1)
                copy_y(2 * t + 1, 1)
            copy_y(B - 2, 0, B - 2)

        @block.vector
        def _(dve):
            def permute(dst, src):
                dve.tensor_copy(dst.rearrange("p (j i c) -> p j i c", j=2, i=2),
                                src.rearrange("p (i j c) -> p j i c", i=2, j=2)).then_inc(permuted, 1)

            dve.wait_ge(const_step, 4)
            permute(ident_ph[:, :], ident[:, :])
            dve.wait_ge(wp_loaded, 16)
            for k in range(3):
                permute(wp_ph[:, k, :], wp_sb[:, k * P:(k + 1) * P])
            dve.wait_ge(coef_ready, 1)
            dve.tensor_copy(coef[:, :], COEF_PS).then_inc(coef_copied, 1)

            def bn(t):
                dve.wait_ge(x_loaded[t], 64)
                for q in range(4):
                    rows = X[:, t, q * PH // 4:(q + 1) * PH // 4, :].rearrange("p h w -> p (h w)")
                    dve.bn_stats(st[:, t, q, :], rows).then_inc(bn_done, 1)

            def aggregate(t):
                dve.wait_ge(bn_done, 4 * t + 4)
                dve.bn_aggr(agg[:, t, :], st[:, t, :, :].rearrange("p q s -> p (q s)")).then_inc(agg_done, 1)

            def variance(n, a, b):
                dve.wait_ge(comb_done, n)
                dve.tensor_tensor(dev[:, a:b], agg[:, a:b, 0], COMB[:, a:b, 0], ALU.subtract).then_inc(stat_step_in, 1)
                dve.wait_ge(stat_step_in, 2 * n - 1)
                dve.tensor_tensor(dev2[:, a:b], dev[:, a:b], dev[:, a:b], ALU.mult).then_inc(stat_step_in, 1)
                dve.wait_ge(stat_step_in, 2 * n)
                dve.scalar_tensor_tensor(vare[:, a:b], dev2[:, a:b], EPS, COMB[:, a:b, 1],
                                         ALU.add, ALU.add).then_inc(stat_step, 1)

            def bias(n, a, b):
                dve.wait_ge(rstd_done, n)
                dve.scalar_tensor_tensor(nbias[:, a:b], COMB[:, a:b, 0], -1.0, rstd[:, a:b],
                                         ALU.mult, ALU.mult).then_inc(stats_ready, 1)

            bn(0)
            aggregate(0)
            variance(1, 0, 1)
            bias(1, 0, 1)
            dve.wait_ge(wpT_ready, 3)
            dve.wait_ge(coef_copied, 1)
            for n, tap in enumerate(INNER):
                dve.wait_ge(w5_scaled, n + 1)
                dve.scalar_tensor_tensor(weff[:, n, :], wpT[:, 1, :], coef[:, w3_col(tap):w3_col(tap) + 1],
                                         weff[:, n, :], ALU.mult, ALU.add).then_inc(weff_step, 1)
            dve.wait_ge(weff_step, 1)
            dve.scalar_tensor_tensor(weff[:, 0, :], wpT[:, 0, :], coef[:, W1_AT:W1_AT + 1],
                                     weff[:, 0, :], ALU.mult, ALU.add).then_inc(weff_step, 1)
            dve.wait_ge(whi_ready, 1)
            dve.tensor_tensor(wlo[:, :, :], weff[:, :, :], whi[:, :, :].bitcast(F32),
                              ALU.subtract).then_inc(wlo_ready, 1)

            def chain_step(b, par, k, first=False):
                tap = DVE_TAPS[k]
                if k == 0:
                    dve.wait_ge(g_ready, 2 * b + 2)
                    if first:
                        dve.tensor_scalar(ACC[:, :, :], g_tap(par, tap, True), of5(tap), None,
                                          ALU.mult).then_inc(acc_step, 1)
                        return
                    dve.wait_ge(f_ready, b)
                    dve.wait_ge(prod_added, N_PROD * (b + 1))
                    dve.scalar_tensor_tensor(ACC[:, :, :], g_tap(par, tap, True), of5(tap), PSUMED[:, par, :, :],
                                             ALU.mult, ALU.add).then_inc(acc_step, 1)
                    return
                dve.wait_ge(acc_step, N_STEP * b + k)
                if k < N_STEP:
                    dve.scalar_tensor_tensor(part(ACC, tap), g_tap(par, tap), of5(tap), part(ACC, tap),
                                             ALU.mult, ALU.add).then_inc(acc_step, 1)
                elif first:
                    dve.scalar_tensor_tensor(part(ACC, tap), g_tap(par, tap), of5(tap), part(ACC, tap),
                                             ALU.mult, ALU.add).then_inc(acc0_done, 1)
                    dve.wait_ge(acc0_done, 1)
                    dve.wait_ge(prod_added, N_PROD)
                    dve.tensor_tensor(F[:, par, :].rearrange("p (h w) -> p h w", w=PW), ACC[:, :, :],
                                      PSUMED[:, par, :, :], ALU.add).then_inc(f_ready, 1)
                else:
                    dve.wait_ge(conv_done, b - 1)
                    dve.scalar_tensor_tensor(F[:, par, :].rearrange("p (h w) -> p h w", w=PW),
                                             g_tap(par, tap, True), of5(tap), ACC[:, :, :],
                                             ALU.mult, ALU.add).then_inc(f_ready, 1)

            def chain(b, par):
                for k in range(N_DVE):
                    chain_step(b, par, k)

            between = {1: lambda: bn(1), 2: lambda: (aggregate(1), bn(2)), 3: lambda: (aggregate(2), bn(3)),
                       4: lambda: aggregate(3), 6: lambda: variance(2, 1, PAIRS), 7: lambda: bias(2, 1, PAIRS)}
            for k in range(N_DVE):
                chain_step(0, 0, k, True)
                if k in between:
                    between[k]()
            chain(1, 1)
            with dve.Fori(0, PAIRS - 1) as t:
                chain(2 * t + 2, 0)
                chain(2 * t + 3, 1)
            dve.wait_ge(conv_done, B)
            for half in range(2):
                r0 = half * BANK_ROWS
                for j in range(2):
                    xr = X[HALF:P, PAIRS - 1, r0:r0 + BANK_ROWS, :].rearrange("p h (w j) -> p h w j", j=2)[:, :, :, j]
                    yr = YP[HALF * j:HALF * (j + 1), 1, r0 * PW:(r0 + BANK_ROWS) * PW].rearrange("p (h w) -> p h w", w=PW)
                    dve.tensor_tensor(xr, yr, xr, ALU.add).then_inc(last_added, 1)

        @block.tensor
        def _(pe):
            pe.wait_ge(const_step, 4)
            for k in range(3):
                pe.wait_ge(permuted, k + 2)
                mm = nc.tensor.transpose(WT_PS[:, k * P:(k + 1) * P], wp_ph[:, k, :], ident[:, :])
            mm.then_inc(wt_ready, 1)
            pe.wait_ge(w_loaded, 48)
            nc.tensor.matmul(COEF_PS, ident_ph[:, :], w_sb[:, :],
                             start=True, stop=True).then_inc(coef_ready, 1)

            def combine(n, a, b):
                pe.wait_ge(const_step, 6)
                pe.wait_ge(agg_done, b)
                nc.tensor.matmul(COMB[:, a:b, :].rearrange("p t s -> p (t s)"), avg[:, :],
                                 agg[:, a:b, :].rearrange("p t s -> p (t s)"),
                                 start=True, stop=True).then_inc(comb_done, 1)

            def tap_matmuls(par, n, w, tile, start=False):
                dy, dx = PE_TAPS[n]
                c0, c1 = (0, PW) if abs(dx) < 2 else span(dx, 0, PW)
                for bank in range(BANKS):
                    r0, r1 = span(dy, bank * BANK_ROWS, (bank + 1) * BANK_ROWS)
                    at = (r0 + dy) * PITCH + 2 + dx
                    src = tile[:, par, at:at + (r1 - r0) * PITCH].rearrange("p (r c) -> p r c", c=PITCH)[:, :, c0:c1]
                    dst = YP[:, par, r0 * PW:r1 * PW].rearrange("p (r c) -> p r c", c=PW)[:, :, c0:c1]
                    mm = nc.tensor.matmul(dst, w[:, n, :], src, start=start, stop=False, skip_group_check=True)
                return mm

            def high(b, par, first=False):
                pe.wait_ge(hi_ready, b + 1)
                if not first:
                    pe.wait_ge(y_copied, 2 * (b - 1))
                for n in range(N_PE):
                    tap_matmuls(par, n, whi, HI, start=(n == 0))
                if first and par == 0:
                    pe.wait_ge(wlo_ready, 1)
                for n in range(N_PE):
                    tap_matmuls(par, n, wlo, HI)

            def low(b, par):
                pe.wait_ge(lo_ready, b + 1)
                for n in range(N_PE):
                    mm = tap_matmuls(par, n, whi, LO)
                mm.then_inc(inner_done, 1)

            def ring(b, par):
                pe.wait_ge(f_ready, b + 1)
                for bank in range(BANKS):
                    cols = slice(bank * 512, (bank + 1) * 512)
                    mm = nc.tensor.matmul(YP[:, par, cols], wpT[:, 2, :], F[:, par, cols],
                                          start=False, stop=True, skip_group_check=True)
                mm.then_inc(conv_done, 1)

            combine(1, 0, 1)
            pe.wait_ge(whi_ready, 1)
            high(0, 0, True)
            combine(2, 1, PAIRS)
            low(0, 0)
            high(1, 1, True)
            ring(0, 0)
            low(1, 1)
            with pe.Fori(0, PAIRS - 1) as t:
                high(2 * t + 2, 0)
                ring(2 * t + 1, 1)
                low(2 * t + 2, 0)
                high(2 * t + 3, 1)
                ring(2 * t + 2, 0)
                low(2 * t + 3, 1)
            ring(B - 1, 1)


_INS = ["x", "L0_conv_w1", "L0_conv_w3", "L0_conv_w5", "L0_conv_w_proj"]


def kernel(**inputs):
    import numpy as _np
    import concourse.bacc as _bacc
    from concourse import mybir as _mybir
    from concourse.bass_utils import run_bass_kernel_spmd as _run

    nc = _bacc.Bacc("TRN2", target_bir_lowering=False, num_devices=1)
    arrays, args = {}, []
    for name in _INS:
        a = _np.ascontiguousarray(inputs[name])
        arrays[f"in_{name}_dram"] = a
        args.append(nc.dram_tensor(f"in_{name}_dram", a.shape, _mybir.dt.from_np(a.dtype), kind="ExternalInput").ap())
    args.append(nc.dram_tensor("out_dram", (B, C, H, W), F32, kind="ExternalOutput").ap())
    build(nc, *args)
    r = _run(nc, [arrays], core_ids=[0])
    return r.results[0]["out_dram"]
```

```python
from contextlib import ExitStack

import concourse.bass as bass
from concourse import mybir

ALU = mybir.AluOpType
ACT = mybir.ActivationFunctionType
F32 = mybir.dt.float32
F32R = mybir.dt.float32r

B, C, H, W = 8, 32, 64, 64
PH, PW = H // 2, W // 2
P = 4 * C
HALF = P // 2
PAIRS = B // 2
EPS = 1e-5
BANK_ROWS = 512 // PW
BANKS = PH // BANK_ROWS

PITCH = PW + 2
G_ROWS = PH + 4
G_SIZE = G_ROWS * PITCH + 4
S_SIZE = PH * PITCH + 4

INNER = [(0, 0)] + [(dy, dx) for dy in (-1, 0, 1) for dx in (-1, 0, 1) if (dy, dx) != (0, 0)]
RING = [(dy, dx) for dy in range(-2, 3) for dx in range(-2, 3) if max(abs(dy), abs(dx)) == 2]
EXTRA = [(1, 2), (-1, 2), (1, -2)]
EXTRA_OF = {0: EXTRA, B - 1: EXTRA[:2]}
POOL_OF = [[(0, 2), (-2, -2), (-2, 2), (2, -2), (2, 2)] + EXTRA[2:] * (b == B - 1) for b in range(B)]
DVE_FIRST = (0, -2)
DVE_OF = [[DVE_FIRST] + [t for t in RING if t not in POOL_OF[b] + EXTRA_OF.get(b, []) + [DVE_FIRST]]
          for b in range(B)]
PE_TAPS = INNER + EXTRA
N_INNER, N_PE = len(INNER), len(PE_TAPS)
N_PROD = [len(taps) - 1 for taps in POOL_OF]
PROD_SIZE = max((PH - abs(dy)) * (PW - abs(dx)) for taps in POOL_OF for dy, dx in taps[1:])
LATE = (0, 1)
N_PADS = 7
SUMS = 3
SLOTS = 4


def products_before(b):
    return sum(N_PROD[:b])


def steps_before(b):
    return sum(len(DVE_OF[n]) - 1 for n in range(b))


def w5_col(tap):
    return (tap[0] + 2) * 5 + tap[1] + 2


W3_AT, W1_AT = 25, 34
N_COEF = 35


def w3_col(tap):
    return W3_AT + (tap[0] + 1) * 3 + tap[1] + 1


def span(d, lo, hi):
    return max(lo, -d), min(hi, PH - d)


def build(nc, x, w1, w3, w5, wp, out):
    with ExitStack() as ctx:
        def sb(name, shape, dt):
            return ctx.enter_context(nc.sbuf_tensor(name, shape, dt))

        def ps(name, shape):
            return ctx.enter_context(nc.psum_tensor(name, shape, F32))

        def sem(name):
            return ctx.enter_context(nc.semaphore(name))

        X = sb("X", [P, PAIRS, PH, W], F32)
        Y = sb("Y", [P, 2, PH, PW, 2], F32)
        G = sb("G", [P, SLOTS, G_SIZE], F32)
        HI = sb("HI", [P, SLOTS, S_SIZE], F32R)
        LO = sb("LO", [P, SLOTS, S_SIZE], F32R)
        RING_SUM = sb("RING_SUM", [P, SUMS, PH, PW], F32)
        PROD = sb("PROD", [P, 2, max(N_PROD), PROD_SIZE], F32)
        F = sb("F", [P, 2, PH * PW], F32)
        wp_sb = sb("wp_sb", [P, 3 * P], F32)
        w_sb = sb("w_sb", [P, N_COEF], F32)
        coef = sb("coef", [P, N_COEF], F32)
        wpT = sb("wpT", [P, 3, P], F32)
        weff = sb("weff", [P, N_PE, P], F32)
        whi = sb("whi", [P, N_PE, P], F32R)
        wlo = sb("wlo", [P, N_PE, P], F32R)
        ident = sb("ident", [P, P], F32)
        ident_ph = sb("ident_ph", [P, P], F32)
        wp_ph = sb("wp_ph", [P, 3, P], F32)
        avg = sb("avg", [P, P], F32)
        mhalf = sb("mhalf", [P, PAIRS], F32)
        st = sb("st", [P, PAIRS, 4, 6], F32)
        agg = sb("agg", [P, PAIRS, 2], F32)
        dev = sb("dev", [P, PAIRS], F32)
        dev2 = sb("dev2", [P, PAIRS], F32)
        vare = sb("vare", [P, PAIRS], F32)
        rstd = sb("rstd", [P, PAIRS], F32)
        nbias = sb("nbias", [P, PAIRS], F32)

        YP = ps("YP", [P, 2, PH * PW])
        ACC = ps("ACC", [P, PH, PW])
        WT_PS = ps("WT_PS", [P, 512])
        SMALL = ps("SMALL", [P, 512])
        COEF_PS = SMALL[:, 0:N_COEF]
        COMB = SMALL[:, 40:40 + 2 * PAIRS].rearrange("p (t s) -> p t s", s=2)

        x_loaded = [sem(f"x_loaded{t}") for t in range(PAIRS)]
        x_top = sem("x_top")
        wp_loaded, w_loaded = sem("wp_loaded"), sem("w_loaded")
        const_step, pads_zero = sem("const_step"), sem("pads_zero")
        permuted = sem("permuted")
        wt_ready, coef_ready = sem("wt_ready"), sem("coef_ready")
        wpT_ready, coef_copied = sem("wpT_ready"), sem("coef_copied")
        w5_scaled, weff_step = sem("w5_scaled"), sem("weff_step")
        whi_ready, wlo_ready, extra_ready = sem("whi_ready"), sem("wlo_ready"), sem("extra_ready")
        extra_low_ready = sem("extra_low_ready")
        bn_done, agg_done, comb_done = sem("bn_done"), sem("agg_done"), sem("comb_done")
        stat_step, rstd_done, stats_ready = sem("stat_step"), sem("rstd_done"), sem("stats_ready")
        stat_step_in = sem("stat_step_in")
        g_ready, hi_ready, lo_ready = sem("g_ready"), sem("hi_ready"), sem("lo_ready")
        first_prod, prod_ready, prod_added = sem("first_prod"), sem("prod_ready"), sem("prod_added")
        acc_step, late_done, f_ready = sem("acc_step"), sem("late_done"), sem("f_ready")
        last_bank = sem("last_bank")
        inner_done, conv_done, y_copied = sem("inner_done"), sem("conv_done"), sem("y_copied")
        row_added, last_added, stored = sem("row_added"), sem("last_added"), sem("stored")

        def image(tile, b, at, rows):
            size = rows * PITCH
            return tile[:, b % SLOTS, at:at + size].rearrange("p (r c) -> p r c", c=PITCH)

        def g_image(b):
            return image(G, b, 2 * PITCH, PH)[:, :, 2:PITCH]

        def g_tap(b, tap, full=False):
            dy, dx = tap
            v = image(G, b, (2 + dy) * PITCH + 2 + dx, PH)[:, :, 0:PW]
            (r0, r1), (c0, c1) = ((0, PH), (0, PW)) if full else (span(dy, 0, PH), span(dx, 0, PW))
            return v[:, r0:r1, c0:c1]

        def part(tile, tap):
            (r0, r1), (c0, c1) = span(tap[0], 0, PH), span(tap[1], 0, PW)
            return tile[:, r0:r1, c0:c1]

        def prod(b, k):
            (r0, r1), (c0, c1) = span(POOL_OF[b][k + 1][0], 0, PH), span(POOL_OF[b][k + 1][1], 0, PW)
            return PROD[:, b % 2, k, 0:(r1 - r0) * (c1 - c0)].rearrange("p (r c) -> p r c", c=c1 - c0)

        def s_image(tile, b):
            return image(tile, b, 0, PH)[:, :, 2:PITCH]

        def of5(tap):
            return coef[:, w5_col(tap):w5_col(tap) + 1]

        block = ctx.enter_context(nc.Block())

        def load_x(eng, t, s, r0, r1):
            for par in range(2):
                for i in range(2):
                    p0 = HALF * par + C * i
                    src = x[2 * t + par].rearrange("c (h i) w -> i c h w", i=2)[i]
                    eng.dma_start(X[p0:p0 + C, t, r0:r1, :], src[:, r0:r1, :]).then_inc(s, 16)

        @block.sync
        def _(sp):
            load_x(sp, 0, x_top, 0, PH // 2)
            load_x(sp, 0, x_loaded[0], PH // 2, PH)
            for t in range(1, PAIRS):
                load_x(sp, t, x_loaded[t], 0, PH)

            def store(t, par, half):
                r0 = half * BANK_ROWS
                for i in range(2):
                    p0 = HALF * par + C * i
                    dst = out[2 * t + par].rearrange("c (h i) w -> i c h w", i=2)[i]
                    src = X[p0:p0 + C, t, r0:r0 + BANK_ROWS, :]
                    sp.dma_start(dst[:, r0:r0 + BANK_ROWS, :], src).then_inc(stored, 16)

            for t in range(PAIRS - 1):
                for half in range(2):
                    sp.wait_ge(row_added, 2 * t + half + 1)
                    for par in range(2):
                        store(t, par, half)
            for half in range(2):
                sp.wait_ge(row_added, B - 2 + half + 1)
                store(PAIRS - 1, 0, half)
            for half in range(2):
                sp.wait_ge(last_added, 2 * half + 2)
                store(PAIRS - 1, 1, half)
            sp.wait_ge(stored, 16 * 2 * 2 * B)

        @block.gpsimd
        def _(pool):
            pool.memset(ident[:, :], 0.0).then_inc(const_step, 1)
            pool.memset(avg[:, :], 0.0).then_inc(const_step, 1)
            pool.wait_ge(const_step, 2)
            pool.affine_select(out=ident[:, :], in_=ident[:, :], compare_op=ALU.not_equal, fill=1.0,
                               base=0, pattern=[[-1, P]], channel_multiplier=1).then_inc(const_step, 1)
            pool.affine_select(out=avg[:, :], in_=avg[:, :], compare_op=ALU.not_equal, fill=0.5,
                               base=0, pattern=[[-1, P]], channel_multiplier=1).then_inc(const_step, 1)
            a = avg[:, :].rearrange("p (b i c) -> p b i c", b=2, i=2)
            for i in range(2):
                pool.wait_ge(const_step, 4 + i)
                pool.affine_select(out=a[:, :, i, :], in_=a[:, :, i, :], compare_op=ALU.not_equal, fill=0.5,
                                   base=-C * (1 - i), pattern=[[-HALF, 2], [-1, C]],
                                   channel_multiplier=1).then_inc(const_step, 1)
            pool.memset(mhalf[:, :], -0.5).then_inc(const_step, 1)
            for tile in (HI, LO):
                v = tile[:, :, 0:PH * PITCH].rearrange("p b (r c) -> p b r c", c=PITCH)
                pool.memset(v[:, :, :, 0:2].bitcast(F32), 0.0).then_inc(pads_zero, 1)
                pool.memset(tile[:, :, PH * PITCH:S_SIZE].bitcast(F32), 0.0).then_inc(pads_zero, 1)
            v = G[:, :, 0:G_ROWS * PITCH].rearrange("p b (r c) -> p b r c", c=PITCH)
            pool.memset(v[:, :, 2:PH + 2, 0:2], 0.0).then_inc(pads_zero, 1)
            pool.memset(G[:, :, 0:2 * PITCH], 0.0).then_inc(pads_zero, 1)
            pool.memset(G[:, :, (PH + 2) * PITCH:G_SIZE], 0.0).then_inc(pads_zero, 1)

            def inv_std(n, a, b):
                pool.wait_ge(const_step, 7)
                pool.wait_ge(stat_step, n)
                pool.tensor_tensor(rstd[:, a:b], vare[:, a:b], mhalf[:, a:b], ALU.pow).then_inc(rstd_done, 1)

            def sum_ring(b):
                pool.wait_ge(hi_ready, b + 1)
                if b >= SLOTS:
                    pool.wait_ge(inner_done, b - SLOTS + 1)
                pool.tensor_tensor(s_image(LO, b), g_image(b), s_image(HI, b).bitcast(F32),
                                   ALU.subtract).then_inc(lo_ready, 1)
                pool.wait_ge(first_prod, b + 1)
                for k in range(N_PROD[b]):
                    pool.wait_ge(prod_ready, products_before(b) + k + 1)
                    if k > 0:
                        pool.wait_ge(prod_added, products_before(b) + k)
                    dst = part(RING_SUM[:, b % SUMS, :, :], POOL_OF[b][k + 1])
                    pool.tensor_tensor(dst, dst, prod(b, k), ALU.add).then_inc(prod_added, 1)

            def add_x(t, images=2):
                for half in range(2):
                    rows = slice(half * BANK_ROWS, (half + 1) * BANK_ROWS)
                    pool.wait_ge(y_copied, 2 * (2 * t + images))
                    xr = X[0:HALF * images, t, rows, :].rearrange("p h w -> p (h w)")
                    yr = Y[0:HALF * images, t % 2, rows, :, :].rearrange("p h w j -> p (h w j)")
                    pool.tensor_tensor(xr, xr, yr, ALU.add).then_inc(row_added, 1)

            inv_std(1, 0, 1)
            sum_ring(0)
            pool.wait_ge(extra_ready, 1)
            pool.tensor_tensor(wlo[:, N_INNER:N_PE, :], weff[:, N_INNER:N_PE, :],
                               whi[:, N_INNER:N_PE, :].bitcast(F32), ALU.subtract).then_inc(extra_low_ready, 1)
            inv_std(2, 1, 2)
            for b in range(1, B):
                sum_ring(b)
                if b == 2:
                    inv_std(3, 2, PAIRS)
                if b >= 4 and b % 2 == 0:
                    add_x(b // 2 - 2)
            add_x(PAIRS - 2)
            add_x(PAIRS - 1, 1)

        @block.scalar
        def _(act):
            act.dma_start(wp_sb[:, :], wp.rearrange("o c a b -> o (c a b)")).then_inc(wp_loaded, 16)
            act.dma_start(w_sb[:, 0:W3_AT], w5.rearrange("c a h w -> c (a h w)")).then_inc(w_loaded, 16)
            act.dma_start(w_sb[:, W3_AT:W1_AT], w3.rearrange("c a h w -> c (a h w)")).then_inc(w_loaded, 16)
            act.dma_start(w_sb[:, W1_AT:N_COEF], w1.rearrange("c a h w -> c (a h w)")).then_inc(w_loaded, 16)
            act.wait_ge(wt_ready, 1)
            for k in range(3):
                act.activation(wpT[:, k, :].rearrange("p (j i o) -> p j i o", j=2, i=2),
                               WT_PS[:, k * P:(k + 1) * P].rearrange("p (i j o) -> p j i o", j=2, i=2),
                               ACT.Copy).then_inc(wpT_ready, 1)
            act.wait_ge(wpT_ready, 3)
            act.wait_ge(coef_copied, 1)
            def scale_w5(n0, n1):
                for n in range(n0, n1):
                    act.activation(weff[:, n, :], wpT[:, 2, :], ACT.Copy,
                                   scale=of5(PE_TAPS[n])).then_inc(w5_scaled, 1)

            scale_w5(0, N_INNER)

            def normalise(b):
                if b >= SLOTS:
                    act.wait_ge(f_ready, b - SLOTS + 1)
                    act.wait_ge(lo_ready, b - SLOTS + 1)
                t, p0 = b // 2, HALF * (b % 2)
                rows = X[p0:p0 + HALF, t, :, :].rearrange("p h (w j) -> p h w j", j=2)
                for j in range(2):
                    act.activation(g_image(b)[HALF * j:HALF * (j + 1)], rows[:, :, :, j], ACT.Identity,
                                   bias=nbias[p0:p0 + HALF, t:t + 1],
                                   scale=rstd[p0:p0 + HALF, t:t + 1]).then_inc(g_ready, 1)

            def split(b):
                act.wait_ge(g_ready, 2 * b + 2)
                if b >= SLOTS:
                    act.wait_ge(inner_done, b - SLOTS + 1)
                act.activation(s_image(HI, b), g_image(b), ACT.Copy).then_inc(hi_ready, 1)

            def products(b):
                if b - SUMS in LATE:
                    act.wait_ge(f_ready, b - SUMS + 1)
                elif b > SUMS:
                    act.wait_ge(acc_step, steps_before(b - SUMS) + 1)
                if b >= 2:
                    act.wait_ge(prod_added, products_before(b - 1))
                act.activation(RING_SUM[:, b % SUMS, :, :], g_tap(b, POOL_OF[b][0], True), ACT.Copy,
                               scale=of5(POOL_OF[b][0])).then_inc(first_prod, 1)
                for k in range(N_PROD[b]):
                    act.activation(prod(b, k), g_tap(b, POOL_OF[b][k + 1]), ACT.Copy,
                                   scale=of5(POOL_OF[b][k + 1])).then_inc(prod_ready, 1)

            def copy_y(b):
                act.wait_ge(conv_done, b + 1)
                if b >= 4:
                    act.wait_ge(row_added, 2 * (b // 2 - 1))
                p0 = HALF * (b % 2)
                for j in range(2):
                    act.activation(Y[p0:p0 + HALF, b // 2 % 2, :, :, j],
                                   YP[HALF * j:HALF * (j + 1), b % 2, :].rearrange("p (h w) -> p h w", w=PW),
                                   ACT.Copy).then_inc(y_copied, 1)

            act.wait_ge(pads_zero, N_PADS)
            act.wait_ge(stats_ready, 1)
            normalise(0)
            split(0)
            products(0)
            scale_w5(N_INNER, N_PE)
            act.wait_ge(w5_scaled, N_PE)
            act.activation(whi[:, N_INNER:N_PE, :], weff[:, N_INNER:N_PE, :], ACT.Copy).then_inc(extra_ready, 1)
            for b in range(1, B):
                if b in (2, 4):
                    act.wait_ge(stats_ready, b // 2 + 1)
                normalise(b)
                split(b)
                if b >= 3:
                    copy_y(b - 3)
                products(b)
            copy_y(B - 3)
            copy_y(B - 2)

        @block.vector
        def _(dve):
            def permute(dst, src):
                dve.tensor_copy(dst.rearrange("p (j i c) -> p j i c", j=2, i=2),
                                src.rearrange("p (i j c) -> p j i c", i=2, j=2)).then_inc(permuted, 1)

            dve.wait_ge(const_step, 4)
            permute(ident_ph[:, :], ident[:, :])
            dve.wait_ge(wp_loaded, 16)
            for k in range(3):
                permute(wp_ph[:, k, :], wp_sb[:, k * P:(k + 1) * P])
            dve.wait_ge(coef_ready, 1)
            dve.tensor_copy(coef[:, :], COEF_PS).then_inc(coef_copied, 1)

            def bn(t):
                for q in range(4):
                    if t == 0 and q == 0:
                        dve.wait_ge(x_top, 64)
                    elif t == 0 and q == 2 or q == 0:
                        dve.wait_ge(x_loaded[t], 64)
                    rows = X[:, t, q * PH // 4:(q + 1) * PH // 4, :].rearrange("p h w -> p (h w)")
                    dve.bn_stats(st[:, t, q, :], rows).then_inc(bn_done, 1)

            def aggregate(t):
                dve.wait_ge(bn_done, 4 * t + 4)
                dve.bn_aggr(agg[:, t, :], st[:, t, :, :].rearrange("p q s -> p (q s)")).then_inc(agg_done, 1)

            def variance(n, a, b):
                dve.wait_ge(comb_done, n)
                dve.tensor_tensor(dev[:, a:b], agg[:, a:b, 0], COMB[:, a:b, 0], ALU.subtract).then_inc(stat_step_in, 1)
                dve.wait_ge(stat_step_in, 2 * n - 1)
                dve.tensor_tensor(dev2[:, a:b], dev[:, a:b], dev[:, a:b], ALU.mult).then_inc(stat_step_in, 1)
                dve.wait_ge(stat_step_in, 2 * n)
                dve.scalar_tensor_tensor(vare[:, a:b], dev2[:, a:b], EPS, COMB[:, a:b, 1],
                                         ALU.add, ALU.add).then_inc(stat_step, 1)

            def bias(n, a, b):
                dve.wait_ge(rstd_done, n)
                dve.scalar_tensor_tensor(nbias[:, a:b], COMB[:, a:b, 0], -1.0, rstd[:, a:b],
                                         ALU.mult, ALU.mult).then_inc(stats_ready, 1)

            def add_w3(*taps):
                for n in taps:
                    dve.wait_ge(w5_scaled, n + 1)
                    dve.scalar_tensor_tensor(weff[:, n, :], wpT[:, 1, :], coef[:, w3_col(INNER[n]):w3_col(INNER[n]) + 1],
                                             weff[:, n, :], ALU.mult, ALU.add).then_inc(weff_step, 1)

            dve.wait_ge(wpT_ready, 3)
            dve.wait_ge(coef_copied, 1)
            add_w3(0, 1, 2)
            bn(0)
            aggregate(0)
            add_w3(3, 4)
            variance(1, 0, 1)
            add_w3(5, 6)
            bias(1, 0, 1)
            add_w3(7, 8)
            dve.scalar_tensor_tensor(weff[:, 0, :], wpT[:, 0, :], coef[:, W1_AT:W1_AT + 1],
                                     weff[:, 0, :], ALU.mult, ALU.add).then_inc(weff_step, 1)
            dve.wait_ge(weff_step, N_INNER + 1)
            dve.tensor_copy(whi[:, 0:N_INNER, :], weff[:, 0:N_INNER, :]).then_inc(whi_ready, 1)
            dve.wait_ge(whi_ready, 1)
            dve.tensor_tensor(wlo[:, 0:N_INNER, :], weff[:, 0:N_INNER, :],
                              whi[:, 0:N_INNER, :].bitcast(F32), ALU.subtract).then_inc(wlo_ready, 1)

            def add_tap(b, k):
                tap, last = DVE_OF[b][k], len(DVE_OF[b]) - 1
                steps, f_image = steps_before(b), F[:, b % 2, :].rearrange("p (h w) -> p h w", w=PW)
                if k > 0:
                    dve.wait_ge(acc_step, steps + k)
                if k == 0 and b in LATE:
                    if b > 0:
                        dve.wait_ge(f_ready, b)
                    dve.wait_ge(g_ready, 2 * b + 2)
                    dve.tensor_scalar(ACC[:, :, :], g_tap(b, tap, True), of5(tap), None,
                                      ALU.mult).then_inc(acc_step, 1)
                elif k == 0:
                    dve.wait_ge(f_ready, b)
                    dve.wait_ge(prod_added, products_before(b + 1))
                    dve.scalar_tensor_tensor(ACC[:, :, :], g_tap(b, tap, True), of5(tap), RING_SUM[:, b % SUMS, :, :],
                                             ALU.mult, ALU.add).then_inc(acc_step, 1)
                elif k < last:
                    dve.scalar_tensor_tensor(part(ACC, tap), g_tap(b, tap), of5(tap), part(ACC, tap),
                                             ALU.mult, ALU.add).then_inc(acc_step, 1)
                elif b in LATE:
                    dve.scalar_tensor_tensor(part(ACC, tap), g_tap(b, tap), of5(tap), part(ACC, tap),
                                             ALU.mult, ALU.add).then_inc(late_done, 1)
                    dve.wait_ge(late_done, b + 1)
                    dve.wait_ge(prod_added, products_before(b + 1))
                    dve.tensor_tensor(f_image, ACC[:, :, :], RING_SUM[:, b % SUMS, :, :], ALU.add).then_inc(f_ready, 1)
                else:
                    if b >= 2:
                        dve.wait_ge(conv_done, b - 1)
                    dve.scalar_tensor_tensor(f_image, g_tap(b, tap, True), of5(tap), ACC[:, :, :],
                                             ALU.mult, ALU.add).then_inc(f_ready, 1)

            between = {(0, 1): lambda: bn(1), (0, 2): lambda: aggregate(1), (0, 4): lambda: bn(2),
                       (0, 5): lambda: (aggregate(2), variance(2, 1, 2)), (0, 6): lambda: bias(2, 1, 2),
                       (0, 7): lambda: bn(3), (1, 0): lambda: aggregate(3),
                       (1, 8): lambda: variance(3, 2, PAIRS), (2, 2): lambda: bias(3, 2, PAIRS)}
            for b in range(B):
                for k in range(len(DVE_OF[b])):
                    add_tap(b, k)
                    if (b, k) in between:
                        between[b, k]()
            for half in range(2):
                dve.wait_ge(last_bank, half + 1)
                r0 = half * BANK_ROWS
                for j in range(2):
                    xr = X[HALF:P, PAIRS - 1, r0:r0 + BANK_ROWS, :].rearrange("p h (w j) -> p h w j", j=2)[:, :, :, j]
                    yr = YP[HALF * j:HALF * (j + 1), 1, r0 * PW:(r0 + BANK_ROWS) * PW].rearrange("p (h w) -> p h w", w=PW)
                    dve.tensor_tensor(xr, yr, xr, ALU.add).then_inc(last_added, 1)

        @block.tensor
        def _(pe):
            pe.wait_ge(const_step, 4)
            for k in range(3):
                pe.wait_ge(permuted, k + 2)
                mm = nc.tensor.transpose(WT_PS[:, k * P:(k + 1) * P], wp_ph[:, k, :], ident[:, :])
            mm.then_inc(wt_ready, 1)
            pe.wait_ge(w_loaded, 48)
            nc.tensor.matmul(COEF_PS, ident_ph[:, :], w_sb[:, :],
                             start=True, stop=True).then_inc(coef_ready, 1)

            def combine(n, a, b):
                pe.wait_ge(const_step, 6)
                pe.wait_ge(agg_done, b)
                nc.tensor.matmul(COMB[:, a:b, :].rearrange("p t s -> p (t s)"), avg[:, :],
                                 agg[:, a:b, :].rearrange("p t s -> p (t s)"),
                                 start=True, stop=True).then_inc(comb_done, 1)

            def tap_matmuls(b, n, w, tile, start=False):
                dy, dx = PE_TAPS[n]
                c0, c1 = (0, PW) if abs(dx) < 2 else span(dx, 0, PW)
                for bank in range(BANKS):
                    r0, r1 = span(dy, bank * BANK_ROWS, (bank + 1) * BANK_ROWS)
                    src = image(tile, b, (r0 + dy) * PITCH + 2 + dx, r1 - r0)[:, :, c0:c1]
                    dst = YP[:, b % 2, r0 * PW:r1 * PW].rearrange("p (r c) -> p r c", c=PW)[:, :, c0:c1]
                    mm = nc.tensor.matmul(dst, w[:, n, :], src, start=start, stop=False, skip_group_check=True)
                return mm

            def high(b):
                pe.wait_ge(hi_ready, b + 1)
                if b >= 2:
                    pe.wait_ge(y_copied, 2 * (b - 1))
                for n in range(N_INNER):
                    tap_matmuls(b, n, whi, HI, start=(n == 0))
                if b == 0:
                    pe.wait_ge(wlo_ready, 1)
                for n in range(N_INNER):
                    tap_matmuls(b, n, wlo, HI)

            def low(b):
                pe.wait_ge(lo_ready, b + 1)
                for n in range(N_INNER):
                    mm = tap_matmuls(b, n, whi, LO)
                extra = EXTRA_OF.get(b, [])
                if extra:
                    pe.wait_ge(extra_low_ready, 1)
                for tap in extra:
                    n = PE_TAPS.index(tap)
                    tap_matmuls(b, n, whi, HI)
                    tap_matmuls(b, n, wlo, HI)
                    mm = tap_matmuls(b, n, whi, LO)
                mm.then_inc(inner_done, 1)

            def ring(b):
                pe.wait_ge(f_ready, b + 1)
                for bank in range(BANKS):
                    cols = slice(bank * 512, (bank + 1) * 512)
                    mm = nc.tensor.matmul(YP[:, b % 2, cols], wpT[:, 2, :], F[:, b % 2, cols],
                                          start=False, stop=True, skip_group_check=True)
                    if b == B - 1:
                        mm.then_inc(last_bank, 1)
                if b < B - 1:
                    mm.then_inc(conv_done, 1)

            combine(1, 0, 1)
            pe.wait_ge(whi_ready, 1)
            for b in range(B):
                high(b)
                if b < 2:
                    combine(b + 2, *[(1, 2), (2, PAIRS)][b])
                if b > 0:
                    ring(b - 1)
                low(b)
            ring(B - 1)


_INS = ["x", "L0_conv_w1", "L0_conv_w3", "L0_conv_w5", "L0_conv_w_proj"]


def kernel(**inputs):
    import numpy as _np
    import concourse.bacc as _bacc
    from concourse import mybir as _mybir
    from concourse.bass_utils import run_bass_kernel_spmd as _run

    nc = _bacc.Bacc("TRN2", target_bir_lowering=False, num_devices=1)
    arrays, args = {}, []
    for name in _INS:
        a = _np.ascontiguousarray(inputs[name])
        arrays[f"in_{name}_dram"] = a
        args.append(nc.dram_tensor(f"in_{name}_dram", a.shape, _mybir.dt.from_np(a.dtype), kind="ExternalInput").ap())
    args.append(nc.dram_tensor("out_dram", (B, C, H, W), F32, kind="ExternalOutput").ap())
    build(nc, *args)
    r = _run(nc, [arrays], core_ids=[0])
    return r.results[0]["out_dram"]
```

```python
from contextlib import ExitStack

import concourse.bass as bass
from concourse import mybir

ALU = mybir.AluOpType
ACT = mybir.ActivationFunctionType
F32 = mybir.dt.float32
F32R = mybir.dt.float32r

B, C, H, W = 8, 32, 64, 64
PH, PW = H // 2, W // 2
P = 4 * C
HALF = P // 2
PAIRS = B // 2
EPS = 1e-5
BANK_ROWS = 512 // PW
BANKS = PH // BANK_ROWS

PITCH = PW + 2
G_ROWS = PH + 4
G_SIZE = G_ROWS * PITCH + 4
S_SIZE = PH * PITCH + 4

INNER = [(0, 0)] + [(dy, dx) for dy in (-1, 0, 1) for dx in (-1, 0, 1) if (dy, dx) != (0, 0)]
RING = [(dy, dx) for dy in range(-2, 3) for dx in range(-2, 3) if max(abs(dy), abs(dx)) == 2]
EXTRA = [(1, 2), (-1, 2), (1, -2)]
EXTRA_OF = {0: EXTRA, B - 1: EXTRA[:2]}
POOL_TAPS = [(0, 2), (-2, -2), (-2, 2), (2, -2), (2, 2), (-2, -1)]
POOL_N = [5 if b < 3 else 6 for b in range(B)]
POOL_OF = [POOL_TAPS[:n] for n in POOL_N]
DVE_FIRST = (0, -2)
DVE_OF = [[DVE_FIRST] + [t for t in RING if t not in POOL_OF[b] + EXTRA_OF.get(b, []) + [DVE_FIRST]]
          for b in range(B)]
PE_TAPS = INNER + EXTRA
N_INNER, N_PE = len(INNER), len(PE_TAPS)
N_PROD = [len(taps) - 1 for taps in POOL_OF]
PROD_SIZE = max((PH - abs(dy)) * (PW - abs(dx)) for taps in POOL_OF for dy, dx in taps[1:])
LATE = (0, 1)
ADD_X_AT = [(B - 4, 2), (B - 2, 2), (B - 1, 4)]
N_PADS = 7
PRODS = 10
TOP = BANK_ROWS + 1
WARM = (2, 2)
SUMS = 3
SLOTS = 4


def products_before(b):
    return sum(N_PROD[:b])


def steps_before(b):
    return sum(len(DVE_OF[n]) - 1 for n in range(b))


def w5_col(tap):
    return (tap[0] + 2) * 5 + tap[1] + 2


W3_AT, W1_AT = 25, 34
N_COEF = 35


def w3_col(tap):
    return W3_AT + (tap[0] + 1) * 3 + tap[1] + 1


def span(d, lo, hi):
    return max(lo, -d), min(hi, PH - d)


def build(nc, x, w1, w3, w5, wp, out):
    with ExitStack() as ctx:
        def sb(name, shape, dt):
            return ctx.enter_context(nc.sbuf_tensor(name, shape, dt))

        def ps(name, shape):
            return ctx.enter_context(nc.psum_tensor(name, shape, F32))

        def sem(name):
            return ctx.enter_context(nc.semaphore(name))

        X = sb("X", [P, PAIRS, PH, W], F32)
        Y = sb("Y", [P, 2, PH, PW, 2], F32)
        G = sb("G", [P, SLOTS, G_SIZE], F32)
        HI = sb("HI", [P, SLOTS, S_SIZE], F32R)
        LO = sb("LO", [P, SLOTS, S_SIZE], F32R)
        RING_SUM = sb("RING_SUM", [P, SUMS, PH, PW], F32)
        PROD = sb("PROD", [P, PRODS, PROD_SIZE], F32)
        F = sb("F", [P, 2, PH * PW], F32)
        wp_sb = sb("wp_sb", [P, 3 * P], F32)
        w_sb = sb("w_sb", [P, N_COEF], F32)
        coef = sb("coef", [P, N_COEF], F32)
        wpT = sb("wpT", [P, 3, P], F32)
        weff = sb("weff", [P, N_PE, P], F32)
        whi = sb("whi", [P, N_PE, P], F32R)
        wlo = sb("wlo", [P, N_PE, P], F32R)
        ident = sb("ident", [P, P], F32)
        ident_ph = sb("ident_ph", [P, P], F32)
        wp_ph = sb("wp_ph", [P, 3, P], F32)
        avg = sb("avg", [P, P], F32)
        mhalf = sb("mhalf", [P, PAIRS], F32)
        st = sb("st", [P, PAIRS, 4, 6], F32)
        agg = sb("agg", [P, PAIRS, 2], F32)
        dev = sb("dev", [P, PAIRS], F32)
        dev2 = sb("dev2", [P, PAIRS], F32)
        vare = sb("vare", [P, PAIRS], F32)
        rstd = sb("rstd", [P, PAIRS], F32)
        nbias = sb("nbias", [P, PAIRS], F32)

        YP = ps("YP", [P, 2, PH * PW])
        ACC = ps("ACC", [P, PH, PW])
        WT_PS = ps("WT_PS", [P, 512])
        SMALL = ps("SMALL", [P, 512])
        COEF_PS = SMALL[:, 0:N_COEF]
        COMB = [bank[:, N_COEF + 1:N_COEF + 1 + 2 * PAIRS].rearrange("p (t s) -> p t s", s=2)
                for bank in (SMALL, SMALL, WT_PS, WT_PS)]

        x_loaded = [sem(f"x_loaded{t}") for t in range(PAIRS)]
        x_top = sem("x_top")
        wp_loaded, w_loaded = sem("wp_loaded"), sem("w_loaded")
        const_step, pads_zero = sem("const_step"), sem("pads_zero")
        permuted, g_top, hi_top = sem("permuted"), sem("g_top"), sem("hi_top")
        wt_ready, coef_ready = sem("wt_ready"), sem("coef_ready")
        wpT_ready, coef_copied = sem("wpT_ready"), sem("coef_copied")
        w5_scaled, weff_step = sem("w5_scaled"), sem("weff_step")
        whi_ready, wlo_ready, extra_ready = sem("whi_ready"), sem("wlo_ready"), sem("extra_ready")
        extra_low_ready = sem("extra_low_ready")
        bn_done, agg_done, comb_done = sem("bn_done"), sem("agg_done"), sem("comb_done")
        variance_ready, rstd_done, stats_ready = sem("variance_ready"), sem("rstd_done"), sem("stats_ready")
        dev_step = sem("dev_step")
        g_ready, hi_ready = sem("g_ready"), sem("hi_ready")
        neg_ready = sem("neg_ready")
        lo_ready = [sem(f"lo_ready{b}") for b in range(B)]
        first_prod, prod_ready, prod_added = sem("first_prod"), sem("prod_ready"), sem("prod_added")
        acc_step, late_done, f_ready = sem("acc_step"), sem("late_done"), sem("f_ready")
        last_bank = sem("last_bank")
        low_done, conv_done, y_copied = sem("low_done"), sem("conv_done"), sem("y_copied")
        half_added, last_added, stored = sem("half_added"), sem("last_added"), sem("stored")
        row_added = [sem(f"row_added{t}") for t in range(PAIRS - 1)]

        def image(tile, b, at, rows):
            size = rows * PITCH
            return tile[:, b % SLOTS, at:at + size].rearrange("p (r c) -> p r c", c=PITCH)

        def g_image(b, r0=0, r1=PH):
            return image(G, b, (2 + r0) * PITCH, r1 - r0)[:, :, 2:PITCH]

        def g_tap(b, tap, full=False):
            dy, dx = tap
            v = image(G, b, (2 + dy) * PITCH + 2 + dx, PH)[:, :, 0:PW]
            (r0, r1), (c0, c1) = ((0, PH), (0, PW)) if full else (span(dy, 0, PH), span(dx, 0, PW))
            return v[:, r0:r1, c0:c1]

        def part(tile, tap):
            (r0, r1), (c0, c1) = span(tap[0], 0, PH), span(tap[1], 0, PW)
            return tile[:, r0:r1, c0:c1]

        def prod(b, k):
            dy, dx = POOL_OF[b][k + 1]
            (r0, r1), (c0, c1) = span(dy, 0, PH), span(dx, 0, PW)
            slot = PROD[:, (products_before(b) + k) % PRODS, 0:(r1 - r0) * (c1 - c0)]
            return slot.rearrange("p (r c) -> p r c", c=c1 - c0)

        def s_image(tile, b, r0=0, r1=PH):
            return image(tile, b, r0 * PITCH, r1 - r0)[:, :, 2:PITCH]

        def of5(tap):
            return coef[:, w5_col(tap):w5_col(tap) + 1]

        block = ctx.enter_context(nc.Block())

        def load_x(eng, t, s, r0, r1):
            for par in range(2):
                for i in range(2):
                    p0 = HALF * par + C * i
                    src = x[2 * t + par].rearrange("c (h i) w -> i c h w", i=2)[i]
                    eng.dma_start(X[p0:p0 + C, t, r0:r1, :], src[:, r0:r1, :]).then_inc(s, 16)

        @block.sync
        def _(sp):
            load_x(sp, 0, x_top, 0, PH // 2)
            load_x(sp, 0, x_loaded[0], PH // 2, PH)
            for t in range(1, PAIRS):
                load_x(sp, t, x_loaded[t], 0, PH)

            def store(b, r0, r1):
                t, par = b // 2, b % 2
                for i in range(2):
                    p0 = HALF * par + C * i
                    dst = out[b].rearrange("c (h i) w -> i c h w", i=2)[i]
                    sp.dma_start(dst[:, r0:r1, :], X[p0:p0 + C, t, r0:r1, :]).then_inc(stored, 16)

            for t in range(PAIRS - 1):
                sp.wait_ge(row_added[t], 16)
                store(2 * t, 0, PH)
                store(2 * t + 1, 0, PH)
            for half in range(2):
                sp.wait_ge(half_added, half + 1)
                store(B - 2, half * BANK_ROWS, (half + 1) * BANK_ROWS)
            for half in range(2):
                sp.wait_ge(last_added, 2 * half + 2)
                store(B - 1, half * BANK_ROWS, (half + 1) * BANK_ROWS)
            sp.wait_ge(stored, 16 * (2 * B + 4))

        @block.gpsimd
        def _(pool):
            pool.memset(ident[:, :], 0.0).then_inc(const_step, 1)
            pool.memset(avg[:, :], 0.0).then_inc(const_step, 1)
            pool.wait_ge(const_step, 2)
            pool.affine_select(out=ident[:, :], in_=ident[:, :], compare_op=ALU.not_equal, fill=1.0,
                               base=0, pattern=[[-1, P]], channel_multiplier=1).then_inc(const_step, 1)
            pool.affine_select(out=avg[:, :], in_=avg[:, :], compare_op=ALU.not_equal, fill=0.5,
                               base=0, pattern=[[-1, P]], channel_multiplier=1).then_inc(const_step, 1)
            a = avg[:, :].rearrange("p (b i c) -> p b i c", b=2, i=2)
            for i in range(2):
                pool.wait_ge(const_step, 4 + i)
                pool.affine_select(out=a[:, :, i, :], in_=a[:, :, i, :], compare_op=ALU.not_equal, fill=0.5,
                                   base=-C * (1 - i), pattern=[[-HALF, 2], [-1, C]],
                                   channel_multiplier=1).then_inc(const_step, 1)
            pool.memset(mhalf[:, :], -0.5).then_inc(const_step, 1)
            for tile in (HI, LO):
                v = tile[:, :, 0:PH * PITCH].rearrange("p b (r c) -> p b r c", c=PITCH)
                pool.memset(v[:, :, :, 0:2].bitcast(F32), 0.0).then_inc(pads_zero, 1)
                pool.memset(tile[:, :, PH * PITCH:S_SIZE].bitcast(F32), 0.0).then_inc(pads_zero, 1)
            v = G[:, :, 0:G_ROWS * PITCH].rearrange("p b (r c) -> p b r c", c=PITCH)
            pool.memset(v[:, :, 2:PH + 2, 0:2], 0.0).then_inc(pads_zero, 1)
            pool.memset(G[:, :, 0:2 * PITCH], 0.0).then_inc(pads_zero, 1)
            pool.memset(G[:, :, (PH + 2) * PITCH:G_SIZE], 0.0).then_inc(pads_zero, 1)

            def inv_std(n, a, b):
                pool.wait_ge(const_step, 7)
                pool.wait_ge(variance_ready, n)
                pool.tensor_tensor(rstd[:, a:b], vare[:, a:b], mhalf[:, a:b], ALU.pow).then_inc(rstd_done, 1)

            def sum_ring(b):
                if b == 0:
                    pool.wait_ge(hi_ready, 1)
                    pool.tensor_tensor(s_image(LO, b), g_image(b), s_image(HI, b).bitcast(F32),
                                       ALU.subtract).then_inc(lo_ready[0], 1)
                else:
                    pool.wait_ge(pads_zero, N_PADS)
                    pool.wait_ge(neg_ready, b)
                    at, size = 2 * PITCH + 2, PH * PITCH - 2
                    pool.dma_start(LO[:, b % SLOTS, 2:2 + size].bitcast(F32), G[:, b % SLOTS, at:at + size],
                                   accum_op=ALU.add).then_inc(lo_ready[b], 16)
                pool.wait_ge(first_prod, b + 1)
                for k in range(N_PROD[b]):
                    pool.wait_ge(prod_ready, products_before(b) + k + 1)
                    if k > 0:
                        pool.wait_ge(prod_added, products_before(b) + k)
                    dst = part(RING_SUM[:, b % SUMS, :, :], POOL_OF[b][k + 1])
                    pool.tensor_tensor(dst, dst, prod(b, k), ALU.add).then_inc(prod_added, 1)
                    if (b, k) in ADD_X_AT:
                        add_x(ADD_X_AT.index((b, k)))

            def add_x(t):
                pool.wait_ge(y_copied, 4 * (t + 1))
                pool.dma_start(X[:, t, :, :].rearrange("p h w -> p (h w)"),
                               Y[:, t % 2, :, :, :].rearrange("p h w j -> p (h w j)"),
                               accum_op=ALU.add).then_inc(row_added[t], 16)

            inv_std(1, 0, 1)
            pool.wait_ge(extra_ready, 1)
            pool.tensor_tensor(wlo[:, N_INNER:N_PE, :], weff[:, N_INNER:N_PE, :],
                               whi[:, N_INNER:N_PE, :].bitcast(F32), ALU.subtract).then_inc(extra_low_ready, 1)
            pool.wait_ge(whi_ready, 1)
            pool.tensor_tensor(wlo[:, 0:N_INNER, :], weff[:, 0:N_INNER, :],
                               whi[:, 0:N_INNER, :].bitcast(F32), ALU.subtract).then_inc(wlo_ready, 1)
            sum_ring(0)
            inv_std(2, 1, 2)
            for b in range(1, B):
                sum_ring(b)
                if b == 1:
                    inv_std(3, 2, PAIRS)
            pool.wait_ge(y_copied, 2 * (B - 1))
            for half in range(2):
                rows = slice(half * BANK_ROWS, (half + 1) * BANK_ROWS)
                xr = X[0:HALF, PAIRS - 1, rows, :].rearrange("p h w -> p (h w)")
                yr = Y[0:HALF, (PAIRS - 1) % 2, rows, :, :].rearrange("p h w j -> p (h w j)")
                pool.tensor_tensor(xr, xr, yr, ALU.add).then_inc(half_added, 1)

        @block.scalar
        def _(act):
            act.dma_start(wp_sb[:, :], wp.rearrange("o c a b -> o (c a b)")).then_inc(wp_loaded, 16)
            act.dma_start(w_sb[:, 0:W3_AT], w5.rearrange("c a h w -> c (a h w)")).then_inc(w_loaded, 16)
            act.dma_start(w_sb[:, W3_AT:W1_AT], w3.rearrange("c a h w -> c (a h w)")).then_inc(w_loaded, 16)
            act.dma_start(w_sb[:, W1_AT:N_COEF], w1.rearrange("c a h w -> c (a h w)")).then_inc(w_loaded, 16)
            act.wait_ge(wt_ready, 1)
            for k in range(3):
                act.activation(wpT[:, k, :].rearrange("p (j i o) -> p j i o", j=2, i=2),
                               WT_PS[:, k * P:(k + 1) * P].rearrange("p (i j o) -> p j i o", j=2, i=2),
                               ACT.Copy).then_inc(wpT_ready, 1)
            act.wait_ge(wpT_ready, 3)
            act.wait_ge(coef_copied, 1)
            for n in range(N_PE):
                act.activation(weff[:, n, :], wpT[:, 2, :], ACT.Copy,
                               scale=of5(PE_TAPS[n])).then_inc(w5_scaled, 1)
            act.wait_ge(w5_scaled, N_PE)
            act.activation(whi[:, N_INNER:N_PE, :], weff[:, N_INNER:N_PE, :], ACT.Copy).then_inc(extra_ready, 1)

            def normalise(b, r0, r1, done):
                if b >= SLOTS:
                    act.wait_ge(f_ready, b - SLOTS + 1)
                    act.wait_ge(lo_ready[b - SLOTS], 16 if b > SLOTS else 1)
                t, p0 = b // 2, HALF * (b % 2)
                rows = X[p0:p0 + HALF, t, r0:r1, :].rearrange("p h (w j) -> p h w j", j=2)
                for j in range(2):
                    act.activation(g_image(b, r0, r1)[HALF * j:HALF * (j + 1)], rows[:, :, :, j], ACT.Identity,
                                   bias=nbias[p0:p0 + HALF, t:t + 1],
                                   scale=rstd[p0:p0 + HALF, t:t + 1]).then_inc(done, 1)

            def split(b):
                act.wait_ge(g_ready, 2 * b + 2)
                if b >= SLOTS:
                    act.wait_ge(low_done, b - SLOTS + 1)
                act.activation(s_image(HI, b), g_image(b), ACT.Copy).then_inc(hi_ready, 1)
                act.wait_ge(hi_ready, b + 1)
                act.activation(s_image(LO, b), s_image(HI, b).bitcast(F32), ACT.Copy,
                               scale=-1.0).then_inc(neg_ready, 1)

            def products(b):
                if b - SUMS in LATE:
                    act.wait_ge(f_ready, b - SUMS + 1)
                elif b > SUMS:
                    act.wait_ge(acc_step, steps_before(b - SUMS) + 1)
                act.activation(RING_SUM[:, b % SUMS, :, :], g_tap(b, POOL_OF[b][0], True), ACT.Copy,
                               scale=of5(POOL_OF[b][0])).then_inc(first_prod, 1)
                for k in range(N_PROD[b]):
                    if products_before(b) + k >= PRODS:
                        act.wait_ge(prod_added, products_before(b) + k - PRODS + 1)
                    act.activation(prod(b, k), g_tap(b, POOL_OF[b][k + 1]), ACT.Copy,
                                   scale=of5(POOL_OF[b][k + 1])).then_inc(prod_ready, 1)

            def copy_y(b):
                act.wait_ge(conv_done, b + 1)
                if b >= 4:
                    act.wait_ge(row_added[b // 2 - 2], 16)
                p0 = HALF * (b % 2)
                for j in range(2):
                    act.activation(Y[p0:p0 + HALF, b // 2 % 2, :, :, j],
                                   YP[HALF * j:HALF * (j + 1), b % 2, :].rearrange("p (h w) -> p h w", w=PW),
                                   ACT.Copy).then_inc(y_copied, 1)

            act.wait_ge(pads_zero, N_PADS)
            act.wait_ge(stats_ready, 1)
            normalise(0, 0, TOP, g_top)
            act.wait_ge(g_top, 2)
            act.activation(s_image(HI, 0, 0, TOP), g_image(0, 0, TOP), ACT.Copy).then_inc(hi_top, 1)
            normalise(0, TOP, PH, g_ready)
            act.wait_ge(g_ready, 2)
            act.activation(s_image(HI, 0, TOP, PH), g_image(0, TOP, PH), ACT.Copy).then_inc(hi_ready, 1)
            products(0)
            for b in range(1, B):
                if b >= 3:
                    copy_y(b - 3)
                if b in (2, 4):
                    act.wait_ge(stats_ready, b // 2 + 1)
                normalise(b, 0, PH, g_ready)
                split(b)
                products(b)
            copy_y(B - 3)
            copy_y(B - 2)

        @block.vector
        def _(dve):
            def permute(dst, src):
                dve.tensor_copy(dst.rearrange("p (j i c) -> p j i c", j=2, i=2),
                                src.rearrange("p (i j c) -> p j i c", i=2, j=2)).then_inc(permuted, 1)

            dve.wait_ge(const_step, 4)
            permute(ident_ph[:, :], ident[:, :])
            dve.wait_ge(wp_loaded, 16)
            for k in range(3):
                permute(wp_ph[:, k, :], wp_sb[:, k * P:(k + 1) * P])
            dve.wait_ge(coef_ready, 1)
            dve.tensor_copy(coef[:, :], COEF_PS).then_inc(coef_copied, 1)

            def bn(t, q0=0, q1=4):
                for q in range(q0, q1):
                    if t == 0 and q == 0:
                        dve.wait_ge(x_top, 64)
                    elif t == 0 and q == 2 or q == 0:
                        dve.wait_ge(x_loaded[t], 64)
                    rows = X[:, t, q * PH // 4:(q + 1) * PH // 4, :].rearrange("p h w -> p (h w)")
                    dve.bn_stats(st[:, t, q, :], rows).then_inc(bn_done, 1)

            def aggregate(t):
                dve.wait_ge(bn_done, 4 * t + 4)
                dve.bn_aggr(agg[:, t, :], st[:, t, :, :].rearrange("p q s -> p (q s)")).then_inc(agg_done, 1)

            def variance(n, a, b):
                dve.wait_ge(comb_done, n)
                dve.tensor_tensor(dev[:, a:b], agg[:, a:b, 0], COMB[a][:, a:b, 0],
                                  ALU.subtract).then_inc(dev_step, 1)
                dve.wait_ge(dev_step, 2 * n - 1)
                dve.tensor_tensor(dev2[:, a:b], dev[:, a:b], dev[:, a:b], ALU.mult).then_inc(dev_step, 1)
                dve.wait_ge(dev_step, 2 * n)
                dve.scalar_tensor_tensor(vare[:, a:b], dev2[:, a:b], EPS, COMB[a][:, a:b, 1],
                                         ALU.add, ALU.add).then_inc(variance_ready, 1)

            def bias(n, a, b):
                dve.wait_ge(rstd_done, n)
                dve.scalar_tensor_tensor(nbias[:, a:b], COMB[a][:, a:b, 0], -1.0, rstd[:, a:b],
                                         ALU.mult, ALU.mult).then_inc(stats_ready, 1)

            def add_w3(*taps):
                for n in taps:
                    dve.wait_ge(w5_scaled, n + 1)
                    col = w3_col(INNER[n])
                    dve.scalar_tensor_tensor(weff[:, n, :], wpT[:, 1, :], coef[:, col:col + 1],
                                             weff[:, n, :], ALU.mult, ALU.add).then_inc(weff_step, 1)

            dve.wait_ge(wpT_ready, 3)
            dve.wait_ge(coef_copied, 1)
            bn(0, 0, 2)
            add_w3(0, 1, 2)
            bn(0, 2, 4)
            aggregate(0)
            add_w3(3, 4)
            variance(1, 0, 1)
            add_w3(5, 6)
            bias(1, 0, 1)
            add_w3(7, 8)
            dve.scalar_tensor_tensor(weff[:, 0, :], wpT[:, 0, :], coef[:, W1_AT:W1_AT + 1],
                                     weff[:, 0, :], ALU.mult, ALU.add).then_inc(weff_step, 1)
            dve.wait_ge(weff_step, N_INNER + 1)
            dve.tensor_copy(whi[:, 0:N_INNER, :], weff[:, 0:N_INNER, :]).then_inc(whi_ready, 1)
            bn(1)

            def add_tap(b, k):
                tap, last = DVE_OF[b][k], len(DVE_OF[b]) - 1
                steps, f_image = steps_before(b), F[:, b % 2, :].rearrange("p (h w) -> p h w", w=PW)
                if k > 0:
                    dve.wait_ge(acc_step, steps + k)
                if k == 0 and b in LATE:
                    if b > 0:
                        dve.wait_ge(f_ready, b)
                    dve.wait_ge(g_ready, 2 * b + 2)
                    dve.tensor_scalar(ACC[:, :, :], g_tap(b, tap, True), of5(tap), None,
                                      ALU.mult).then_inc(acc_step, 1)
                elif k == 0:
                    dve.wait_ge(f_ready, b)
                    dve.wait_ge(prod_added, products_before(b + 1))
                    dve.scalar_tensor_tensor(ACC[:, :, :], g_tap(b, tap, True), of5(tap), RING_SUM[:, b % SUMS, :, :],
                                             ALU.mult, ALU.add).then_inc(acc_step, 1)
                elif k < last:
                    dve.scalar_tensor_tensor(part(ACC, tap), g_tap(b, tap), of5(tap), part(ACC, tap),
                                             ALU.mult, ALU.add).then_inc(acc_step, 1)
                elif b in LATE:
                    dve.scalar_tensor_tensor(part(ACC, tap), g_tap(b, tap), of5(tap), part(ACC, tap),
                                             ALU.mult, ALU.add).then_inc(late_done, 1)
                    dve.wait_ge(late_done, LATE.index(b) + 1)
                    if b >= 2:
                        dve.wait_ge(conv_done, b - 1)
                    dve.wait_ge(prod_added, products_before(b + 1))
                    dve.tensor_tensor(f_image, ACC[:, :, :], RING_SUM[:, b % SUMS, :, :],
                                      ALU.add).then_inc(f_ready, 1)
                else:
                    if b >= 2:
                        dve.wait_ge(conv_done, b - 1)
                    dve.scalar_tensor_tensor(f_image, g_tap(b, tap, True), of5(tap), ACC[:, :, :],
                                             ALU.mult, ALU.add).then_inc(f_ready, 1)

            def statistics_after(b, k):
                if (b, k) == (0, 0):
                    aggregate(1)
                if (b, k) == (0, 2):
                    bn(2)
                    aggregate(2)
                if (b, k) == (0, 3):
                    variance(2, 1, 2)
                if (b, k) == (0, 4):
                    bn(3)
                if (b, k) == (0, 5):
                    bias(2, 1, 2)
                if (b, k) == (0, 6):
                    aggregate(3)
                if (b, k) == (0, 7):
                    variance(3, 2, PAIRS)
                if (b, k) == (1, 5):
                    bias(3, 2, PAIRS)

            for b in range(B):
                for k in range(len(DVE_OF[b])):
                    add_tap(b, k)
                    statistics_after(b, k)
            for half in range(2):
                dve.wait_ge(last_bank, half + 1)
                r0 = half * BANK_ROWS
                for j in range(2):
                    xr = X[HALF:P, PAIRS - 1, r0:r0 + BANK_ROWS, :]
                    xr = xr.rearrange("p h (w j) -> p h w j", j=2)[:, :, :, j]
                    yr = YP[HALF * j:HALF * (j + 1), 1, r0 * PW:(r0 + BANK_ROWS) * PW]
                    yr = yr.rearrange("p (h w) -> p h w", w=PW)
                    dve.tensor_tensor(xr, yr, xr, ALU.add).then_inc(last_added, 1)

        @block.tensor
        def _(pe):
            pe.wait_ge(const_step, 4)
            for k in range(3):
                pe.wait_ge(permuted, k + 2)
                mm = nc.tensor.transpose(WT_PS[:, k * P:(k + 1) * P], wp_ph[:, k, :], ident[:, :])
            mm.then_inc(wt_ready, 1)
            pe.wait_ge(w_loaded, 48)
            nc.tensor.matmul(COEF_PS, ident_ph[:, :], w_sb[:, :],
                             start=True, stop=True).then_inc(coef_ready, 1)

            def combine(n, a, b):
                pe.wait_ge(const_step, 6)
                pe.wait_ge(agg_done, b)
                nc.tensor.matmul(COMB[a][:, a:b, :].rearrange("p t s -> p (t s)"), avg[:, :],
                                 agg[:, a:b, :].rearrange("p t s -> p (t s)"),
                                 start=True, stop=True).then_inc(comb_done, 1)

            def tap_matmuls(b, n, w, tile, start=False, banks=range(BANKS)):
                dy, dx = PE_TAPS[n]
                c0, c1 = (0, PW) if abs(dx) < 2 else span(dx, 0, PW)
                for bank in banks:
                    r0, r1 = span(dy, bank * BANK_ROWS, (bank + 1) * BANK_ROWS)
                    src = image(tile, b, (r0 + dy) * PITCH + 2 + dx, r1 - r0)[:, :, c0:c1]
                    dst = YP[:, b % 2, r0 * PW:r1 * PW].rearrange("p (r c) -> p r c", c=PW)[:, :, c0:c1]
                    mm = nc.tensor.matmul(dst, w[:, n, :], src, start=start, stop=False, skip_group_check=True)
                return mm

            def high(b):
                if b == 0:
                    for bank, rows_ready in enumerate([hi_top, hi_ready]):
                        pe.wait_ge(rows_ready, 1)
                        for n in range(N_INNER):
                            tap_matmuls(b, n, whi, HI, start=(n == 0), banks=[bank])
                    combine(2, 1, 2)
                    pe.wait_ge(wlo_ready, 1)
                else:
                    pe.wait_ge(hi_ready, b + 1)
                    if b >= 2:
                        pe.wait_ge(y_copied, 2 * (b - 1))
                    for n in range(N_INNER):
                        tap_matmuls(b, n, whi, HI, start=(n == 0))
                if b == 1:
                    combine(3, 2, PAIRS)
                for n in range(N_INNER):
                    tap_matmuls(b, n, wlo, HI)

            def low(b):
                pe.wait_ge(lo_ready[b], 16 if b > 0 else 1)
                for n in range(N_INNER):
                    mm = tap_matmuls(b, n, whi, LO)
                extra = EXTRA_OF.get(b, [])
                if extra:
                    pe.wait_ge(extra_low_ready, 1)
                for tap in extra:
                    n = PE_TAPS.index(tap)
                    tap_matmuls(b, n, whi, HI)
                    tap_matmuls(b, n, wlo, HI)
                    mm = tap_matmuls(b, n, whi, LO)
                mm.then_inc(low_done, 1)

            def ring(b):
                pe.wait_ge(f_ready, b + 1)
                for bank in range(BANKS):
                    cols = slice(bank * 512, (bank + 1) * 512)
                    mm = nc.tensor.matmul(YP[:, b % 2, cols], wpT[:, 2, :], F[:, b % 2, cols],
                                          start=False, stop=True, skip_group_check=True)
                    if b == B - 1:
                        mm.then_inc(last_bank, 1)
                if b < B - 1:
                    mm.then_inc(conv_done, 1)

            def keep_warm():
                nc.tensor.matmul(YP[:, 0, 0:3 * P], ident[:, :], wp_ph[:, :, :].rearrange("p k o -> p (k o)"),
                                 start=True, stop=True)

            for _ in range(WARM[0]):
                keep_warm()
            combine(1, 0, 1)
            for _ in range(WARM[1]):
                keep_warm()
            pe.wait_ge(whi_ready, 1)
            for b in range(B):
                high(b)
                if b > 0:
                    ring(b - 1)
                low(b)
            ring(B - 1)


_INS = ["x", "L0_conv_w1", "L0_conv_w3", "L0_conv_w5", "L0_conv_w_proj"]


def kernel(**inputs):
    import numpy as _np
    import concourse.bacc as _bacc
    from concourse import mybir as _mybir
    from concourse.bass_utils import run_bass_kernel_spmd as _run

    nc = _bacc.Bacc("TRN2", target_bir_lowering=False, num_devices=1)
    arrays, args = {}, []
    for name in _INS:
        a = _np.ascontiguousarray(inputs[name])
        arrays[f"in_{name}_dram"] = a
        args.append(nc.dram_tensor(f"in_{name}_dram", a.shape, _mybir.dt.from_np(a.dtype), kind="ExternalInput").ap())
    args.append(nc.dram_tensor("out_dram", (B, C, H, W), F32, kind="ExternalOutput").ap())
    build(nc, *args)
    r = _run(nc, [arrays], core_ids=[0])
    return r.results[0]["out_dram"]
```
